# Optimizing a Trainium2 kernel written in Bass

```python
import numpy as np
import jax
import jax.numpy as jnp

def _softmax(x, axis=-1):
    return jax.nn.softmax(x, axis=axis)

def _gelu(x):
    return jax.nn.gelu(x, approximate=True)

def _silu(x):
    return jax.nn.silu(x)

def _sigmoid(x):
    return jax.nn.sigmoid(x)

def _layernorm(x, axis=-1, eps=1e-05):
    m = jnp.mean(x, axis=axis, keepdims=True)
    v = jnp.var(x, axis=axis, keepdims=True)
    return (x - m) / jnp.sqrt(v + eps)

def _scatter_add(tgt, idx, src, axis=0):
    return tgt.at[idx].add(src)

def _segment_sum(src, seg, n):
    return jax.ops.segment_sum(src, seg, n)
kernel_name = 'mk_sandwich_d1_jaxref_r8_3c449b'

def setup_inputs(seed: int=0):
    np.random.seed(seed)
    _w = jnp.asarray

    def _L0_attn_setup():
        import jax, jax.numpy as jnp
        import numpy as np
        DIM = 128
        N_HEADS = 16
        N_KV = 4
        HEAD_DIM = DIM // N_HEADS
        GROUP = N_HEADS // N_KV
        KV_DIM = N_KV * HEAD_DIM
        B, S = (2, 256)
        key = jax.random.key(seed)
        ks = jax.random.split(key, 5)
        scale = 1.0 / np.sqrt(DIM)
        return {'x': jax.random.normal(ks[0], (B, S, DIM), dtype=jnp.float32), 'W_qkv': jax.random.normal(ks[1], (DIM, DIM + 2 * KV_DIM), dtype=jnp.float32) * scale, 'b_qkv': jnp.zeros((DIM + 2 * KV_DIM,), dtype=jnp.float32), 'W_out': jax.random.normal(ks[2], (DIM, DIM), dtype=jnp.float32) * scale, 'b_out': jnp.zeros((DIM,), dtype=jnp.float32)}
    _L0_attn_in = _L0_attn_setup()

    def _L0_ffn_setup():
        import jax, jax.numpy as jnp
        import numpy as np
        THRESH_FACTOR = 0.7

        def ternary_quantize(w):
            delta = THRESH_FACTOR * jnp.mean(jnp.abs(w))
            return jnp.where(w > delta, 1.0, jnp.where(w < -delta, -1.0, 0.0)).astype(w.dtype)
        key = jax.random.key(seed)
        k1, k2, k3 = jax.random.split(key, 3)
        B, S, D_IN, D_OUT = (8, 512, 128, 128)
        inp = {'input': jax.random.normal(k1, (B, S, D_IN), dtype=jnp.float32), 'weight': jax.random.normal(k2, (D_OUT, D_IN), dtype=jnp.float32) * (1.0 / np.sqrt(D_IN)), 'alpha': jnp.ones((1,), dtype=jnp.float32), 'bias': jax.random.normal(k3, (D_OUT,), dtype=jnp.float32) * (1.0 / np.sqrt(D_IN))}
        return inp
    _L0_ffn_in = _L0_ffn_setup()
    _d = {'L0_attn_x': _L0_attn_in['x'], 'L0_attn_W_qkv': _L0_attn_in['W_qkv'], 'L0_attn_b_qkv': _L0_attn_in['b_qkv'], 'L0_attn_W_out': _L0_attn_in['W_out'], 'L0_attn_b_out': _L0_attn_in['b_out'], 'L0_ffn_weight': _L0_ffn_in['weight'], 'L0_ffn_alpha': _L0_ffn_in['alpha'], 'L0_ffn_bias': _L0_ffn_in['bias']}
    _x0 = _d['L0_attn_x']
    _d['L0_attn_x'] = jax.random.normal(jax.random.fold_in(jax.random.key(seed), 1), (32, 256, 128), dtype=_x0.dtype)
    del _x0
    return _d

def reference(L0_attn_x, L0_attn_W_qkv, L0_attn_b_qkv, L0_attn_W_out, L0_attn_b_out, L0_ffn_weight, L0_ffn_alpha, L0_ffn_bias):

    def _L0_attn_ref(x, W_qkv, b_qkv, W_out, b_out):
        import jax, jax.numpy as jnp
        import numpy as np
        DIM = 128
        N_HEADS = 16
        N_KV = 4
        HEAD_DIM = DIM // N_HEADS
        GROUP = N_HEADS // N_KV
        KV_DIM = N_KV * HEAD_DIM
        B, S = (2, 256)
        b, s, d = x.shape
        qkv = x @ W_qkv + b_qkv
        q, k, v = jnp.split(qkv, [DIM, DIM + KV_DIM], axis=-1)
        q = q.reshape(b, s, N_HEADS, HEAD_DIM).transpose(0, 2, 1, 3)
        q = q.reshape(b, N_KV, GROUP, s, HEAD_DIM)
        k = k.reshape(b, s, N_KV, HEAD_DIM).transpose(0, 2, 1, 3)
        v = v.reshape(b, s, N_KV, HEAD_DIM).transpose(0, 2, 1, 3)
        scores = jnp.einsum('bkgsd,bktd->bkgst', q, k) / np.sqrt(HEAD_DIM)
        causal = jnp.tril(jnp.ones((s, s), dtype=bool))
        scores = jnp.where(causal, scores, -jnp.inf)
        attn = jax.nn.softmax(scores, axis=-1)
        y = jnp.einsum('bkgst,bktd->bkgsd', attn, v)
        y = y.reshape(b, N_HEADS, s, HEAD_DIM).transpose(0, 2, 1, 3).reshape(b, s, d)
        return y @ W_out + b_out

    def _L0_ffn_ref(input, weight, alpha, bias):
        import jax, jax.numpy as jnp
        import numpy as np
        THRESH_FACTOR = 0.7

        def ternary_quantize(w):
            delta = THRESH_FACTOR * jnp.mean(jnp.abs(w))
            return jnp.where(w > delta, 1.0, jnp.where(w < -delta, -1.0, 0.0)).astype(w.dtype)
        w_ternary = ternary_quantize(weight)
        w_eff = w_ternary * alpha
        out = jnp.einsum('bsd,od->bso', input, w_eff) + bias
        return out
    x = L0_attn_x
    x = x + _layernorm(_L0_attn_ref(_layernorm(x, axis=-1), L0_attn_W_qkv, L0_attn_b_qkv, L0_attn_W_out, L0_attn_b_out), axis=-1)
    x = x + _layernorm(_L0_ffn_ref(_layernorm(x, axis=-1), L0_ffn_weight, L0_ffn_alpha, L0_ffn_bias), axis=-1)
    return x

_drawn_inputs = setup_inputs


def setup_inputs(seed=0):
    import zlib

    import numpy as np

    out = dict(_drawn_inputs(seed))
    spreads = {'L0_attn_b_qkv': (0.0, 0.1), 'L0_attn_b_out': (0.0, 0.1)}
    factors = {'L0_ffn_bias': 8.0}
    for name, (base, spread) in spreads.items():
        noise = np.random.default_rng([zlib.crc32(name.encode()), seed]).standard_normal(out[name].shape)
        drawn = base * np.exp(spread * noise) if base else spread * noise
        out[name] = jnp.asarray(drawn.astype(out[name].dtype))
    for name, factor in factors.items():
        out[name] = (out[name] * factor).astype(out[name].dtype)
    return out
```

```python
from contextlib import ExitStack

import concourse.bass as bass
from concourse import mybir

F32 = mybir.dt.float32
BF16 = mybir.dt.bfloat16
ALU = mybir.AluOpType
ACT = mybir.ActivationFunctionType
AX_X = mybir.AxisListType.X

B, S, D = 32, 256, 128
NH, NKV, HD = 16, 4, 8
G = NH // NKV
NLO = 2
BL = 64
NB = S // BL
TT = S // 128
EPS = 1e-5
SCALE = HD ** -0.5
BIG = 1.0e30
SLOT = G * BL
MAXROW = 6 * HD
RING = 4
GRP = 4
CHUNKS = 6
BANKS = 10
NORM, PROJ, SPLIT, MAX, TURN, ATT, DIV, OUT, MID, FFN = range(10)
STEPS = B + FFN
ON_ACT = (1, 3)
FIRST, LOOPS = 10, 5


class Step:

    def __init__(self, t0, it=None):
        self.t0, self.it = t0, it

    def on(self, lag):
        return 0 <= self.t0 - lag < B

    def b(self, lag):
        return self.t0 - lag

    def n(self, lag, per, more=0):
        v = per * (self.t0 - lag) + more
        return v if self.it is None else self.it * (RING * per) + v

    def group(self, first):
        v = (self.t0 - first) // GRP
        return v if self.it is None else self.it + v


def run_steps(eng, step):
    for t in range(FIRST):
        step(Step(t))
    with eng.Fori(0, LOOPS) as it:
        for j in range(RING):
            step(Step(FIRST + j, it))
    for t in range(FIRST + RING * LOOPS, STEPS):
        step(Step(t))


ST_CHUNKS = [(lo, mats, banks) for lo in range(NLO) for mats, banks in (
    ([(0, True, 0, 1, 0), (0, False, 1, 1, 1), (0, False, 2, 2, 2)], 2),
    ([(3, True, 3, 1, 0), (1, True, 1, 1, 1), (1, False, 2, 2, 2)], 2),
    ([(2, True, 2, 1, 0), (2, False, 3, 1, 1)], 1))]
PV_CHUNKS = [[(0, 0)], [(3, 0), (1, 1)], [(2, 0)]] * NLO
MX_BANKS = [bank for kv in range(0, NKV, 2) for bank in (
    [(kv, 3)], [(kv + 1, 3)], [(kv, 2), (kv, 0)], [(kv + 1, 2), (kv + 1, 0)], [(kv, 1), (kv + 1, 1)])]


def build(nc, x, wq, wk, wv, wo, bq, bk, bo, wf, alpha, bf, ident, qfix, kfix, vmask, bvw, out):
    with ExitStack() as ctx:
        def sb(name, shape, dt):
            return ctx.enter_context(nc.sbuf_tensor(name, shape, dt))

        def psum(name, shape):
            return ctx.enter_context(nc.psum_tensor(name, shape, F32))

        def sem(name):
            return ctx.enter_context(nc.semaphore(name))

        wq_sb = sb("wq_sb", [D, 128], F32)
        wk_sb = sb("wk_sb", [D, 128], F32)
        wv_sb = sb("wv_sb", [D, 32], F32)
        wo_sb = sb("wo_sb", [128, NLO, D], F32)
        bq_sb = sb("bq_sb", [128, 1], F32)
        bk_sb = sb("bk_sb", [128, 1], F32)
        bv_sb = sb("bv_sb", [128, NLO, 128], F32)
        bo_sb = sb("bo_sb", [128, TT, D], F32)
        wf_sb = sb("wf_sb", [D, D], F32)
        al_sb = sb("al_sb", [128, 1], F32)
        bf_sb = sb("bf_sb", [128, TT, D], F32)
        id_sb = sb("id_sb", [128, 128], F32)
        idb = sb("idb", [128, 128], BF16)
        qf_sb = sb("qf_sb", [128, S], F32)
        kf_sb = sb("kf_sb", [128, 2, S], F32)
        qfb = sb("qfb", [128, S], BF16)
        kfb = sb("kfb", [128, 2 * S], BF16)
        vm_sb = sb("vm_sb", [128, 2 * NLO * NB, HD], F32)
        ones = sb("ones", [128, 128], F32)
        zrow = sb("zrow", [2, NH * S], BF16)
        wabs = sb("wabs", [D, D], F32)
        wneg = sb("wneg", [D, D], F32)
        wsum = sb("wsum", [D, 1], F32)
        delta = sb("delta", [D, 2], F32)
        weff = sb("weff", [D, D], F32)

        X = sb("X", [128, B * TT, D], F32)
        xn1 = sb("xn1", [128, TT, D], F32)
        xn1T = sb("xn1T", [128, S], F32)
        QK = sb("QK", [128, 2, S], F32)
        part1 = [sb(f"part1_{i}", [128, 2, S], BF16) for i in range(2)]
        part2 = [sb(f"part2_{i}", [128, 2, S], BF16) for i in range(2)]
        part3 = [sb(f"part3_{i}", [128, 2, S], BF16) for i in range(2)]
        kparts = [sb(f"kparts_{i}", [96, S], BF16) for i in range(2)]
        rest = sb("rest", [128, 2, S], F32)
        QS = [sb(f"QS{i}", [128, NH, S], BF16) for i in range(RING)]
        KS = [sb(f"KS{i}", [128, NKV, 2, S], BF16) for i in range(RING)]
        VB = [sb(f"VB{i}", [128, NB * NLO * 2, 2 * HD], F32) for i in range(RING)]
        M = [sb(f"M{i}", [128, NKV, 2, NB], F32) for i in range(2)]
        Mp = sb("Mp", [128, 2, NKV * 2 * NB], BF16)
        MpT = sb("MpT", [4 * NKV, 2 * S], BF16)
        PT = [sb(f"PT{i}", [128, 1024], F32) for i in range(2)]
        Y = sb("Y", [128, NLO, S], F32)
        den = sb("den", [128, NLO * S // 16], F32)
        rec = sb("rec", [128, NLO * S // 16], F32)
        rec_dram = nc.dram_tensor("rec_dram", [8, NLO * S], F32).ap()
        rden = sb("rden", [128, NLO, S], F32)
        yn = sb("yn", [128, NLO, S], F32)
        A1 = sb("A1", [128, TT, D], F32)
        A2 = sb("A2", [128, TT, D], F32)
        xn3 = sb("xn3", [128, TT, D], F32)
        xn3T = sb("xn3T", [128, S], F32)
        F1 = sb("F1", [128, TT, D], F32)
        F2 = sb("F2", [128, TT, D], F32)
        stats = [sb(f"stats{i}", [128, TT, 6], F32) for i in range(4)]
        mv = [sb(f"mv{i}", [128, TT, 2], F32) for i in range(4)]
        vareps = [sb(f"vareps{i}", [128, TT], F32) for i in range(4)]
        mhalf = sb("mhalf", [128, TT], F32)
        minus = sb("minus", [128, TT], F32)
        eps = sb("eps", [128, TT], F32)
        nmean = [sb(f"nmean{i}", [128, TT], F32) for i in range(4)]
        shift = [sb(f"shift{i}", [128, TT], F32) for i in range(4)]
        rstd = [sb(f"rstd{i}", [128, TT], F32) for i in range(4)]

        ps_st = [psum(f"ps_st{i}", [128, 2, 512]) for i in range(2)]
        ps_mx = [psum(f"ps_mx{i}", [128, 512]) for i in range(2)]
        ps_y = psum("ps_y", [128, NLO, S])
        ps_w = psum("ps_w", [128, 512])

        s_const = sem("s_const")
        s_passed = sem("s_passed")
        s_x = sem("s_x")
        s_store = sem("s_store")
        s_setup = sem("s_setup")
        s_setg = sem("s_setg")
        s_fix = sem("s_fix")
        s_fixed = sem("s_fixed")
        s_bo = sem("s_bo")
        s_wps = sem("s_wps")
        s_wchain = sem("s_wchain")
        s_weff = sem("s_weff")
        s_ln = [sem(f"s_ln{i}") for i in range(4)]
        s_rstd = [sem(f"s_rstd{i}") for i in range(4)]
        s_xn1 = sem("s_xn1")
        s_xt_ps = sem("s_xt_ps")
        s_xt = sem("s_xt")
        s_qk_ps = sem("s_qk_ps")
        s_qk = sem("s_qk")
        s_v_ps = sem("s_v_ps")
        s_vb = sem("s_vb")
        s_p1 = sem("s_p1")
        s_r1 = sem("s_r1")
        s_p2 = sem("s_p2")
        s_p3 = sem("s_p3")
        s_kp = sem("s_kp")
        s_stack = [sem(f"s_stack{i}") for i in range(2)]
        s_mx_ps = sem("s_mx_ps")
        s_mx = sem("s_mx")
        s_mp = sem("s_mp")
        s_mt_ps = sem("s_mt_ps")
        s_mt = sem("s_mt")
        s_mrow = sem("s_mrow")
        s_st_ps = sem("s_st_ps")
        s_exp = sem("s_exp")
        s_pv = sem("s_pv")
        s_y = sem("s_y")
        s_den = sem("s_den")
        s_rec = sem("s_rec")
        s_recd = sem("s_recd")
        s_shift = sem("s_shift")
        s_yn = sem("s_yn")
        s_op_ps = sem("s_op_ps")
        s_a1 = sem("s_a1")
        s_a2 = sem("s_a2")
        s_x1 = sem("s_x1")
        s_xn3 = sem("s_xn3")
        s_x3_ps = sem("s_x3_ps")
        s_x3 = sem("s_x3")
        s_ff_ps = sem("s_ff_ps")
        s_f1 = sem("s_f1")
        s_f2 = sem("s_f2")
        s_fin = sem("s_fin")

        consts = [(wq_sb, wq), (wk_sb, wk), (wv_sb, wv), (wo_sb, wo), (bq_sb, bq), (bk_sb, bk), (bv_sb, bvw),
                  (bo_sb, bo), (wf_sb, wf), (al_sb, alpha), (bf_sb, bf), (id_sb, ident), (kf_sb, kfix),
                  (vm_sb, vmask), (qf_sb, qfix)]
        CONST = 16 * len(consts)
        STACK = 16 * 10
        FIXED = 16 * 2 * RING

        WORK = {"v": (SPLIT, s_vb), "op": (OUT, s_a1), "turn": (TURN, s_mt), "x1": (PROJ, s_xt), "ff": (FFN, s_f1),
                "qk": (PROJ, s_qk), "x3": (MID, s_x3)}
        ORDER = list(WORK)

        def last_work(s, user):
            at = ORDER.index(user)
            for back in range(1, (FFN + 1) * len(ORDER)):
                ago, k = -((at - back) // len(ORDER)), (at - back) % len(ORDER)
                lag, freed = WORK[ORDER[k]]
                if 0 <= s.t0 - ago - lag < B:
                    per = 2 if freed is s_qk else 1
                    return freed, s.n(lag, per, per * (1 - ago))
            return None, 0

        def settle(eng):
            eng.sem_inc(s_passed, 1)

        def stacks_filled(eng, s, lag):
            if s.b(lag) >= 2:
                v = s.b(lag) // 2 * STACK
                eng.wait_ge(s_stack[s.b(lag) % 2], v if s.it is None else s.it * (2 * STACK) + v)

        block = ctx.enter_context(nc.Block())

        @block.sync
        def _(sp):
            xv = x.rearrange("(n b) (j p) d -> n p (b j) d", b=GRP, p=128)
            ov = out.rearrange("(n b) (j p) d -> n p (b j) d", b=GRP, p=128)

            def rows(g):
                return X[:, bass.ds(g * (GRP * TT), GRP * TT), :]

            def load(g):
                sp.dma_start(rows(g), xv[bass.ds(g, 1)].rearrange("n p r d -> (n p) r d")).then_inc(s_x, 16)

            load(0)
            for dst, src in consts:
                sp.dma_start(dst[:], src).then_inc(s_const, 16)
            sp.wait_ge(s_fix, 2)
            for i in range(RING):
                sp.dma_start(QS[i][MAXROW:128], qfb[MAXROW:128, :].unsqueeze(1)
                             .broadcast_to([128 - MAXROW, NH, S])).then_inc(s_fixed, 16)
                sp.dma_start(KS[i][MAXROW:128].rearrange("r h v s -> r h (v s)"), kfb[MAXROW:128, :].unsqueeze(1)
                             .broadcast_to([128 - MAXROW, NKV, 2 * S])).then_inc(s_fixed, 16)
            sp.wait_ge(s_setg, 1)
            sp.wait_ge(s_fixed, FIXED)

            def step(s):
                if s.t0 % GRP == 2 and s.t0 < B - GRP:
                    g = s.group(2 - GRP)
                    sp.wait_ge(s_x, g * 16)
                    settle(sp)
                    load(g)
                if s.on(DIV):
                    sp.wait_ge(s_y, s.n(DIV, 1, 1))
                    if s.b(DIV) >= 1:
                        settle(sp)
                        sp.wait_ge(s_rec, s.n(DIV, 1))
                    sp.dma_start(den[:], Y[HD:128:2 * HD].rearrange("r a s -> r (a s)")).then_inc(s_den, 16)
                if s.on(SPLIT):
                    b = s.b(SPLIT)
                    q, k, i = QS[b % RING], KS[b % RING], b % 2
                    if b >= RING:
                        sp.wait_ge(s_st_ps, s.n(SPLIT, CHUNKS, CHUNKS * (1 - RING)))
                    sp.dma_start(q[MAXROW:MAXROW + 2, :, :], zrow[:, :]).then_inc(s_stack[i], 16)
                    sp.wait_ge(s_p1, s.n(SPLIT, 1, 1))
                    for c in (0, 1, 2):
                        sp.dma_start(q[8 * c:8 * c + 8, :, :], part1[i][:, 0, :]).then_inc(s_stack[i], 16)
                if s.on(SPLIT):
                    sp.wait_ge(s_p2, s.n(SPLIT, 1, 1))
                    for c in (3, 4):
                        sp.dma_start(q[8 * c:8 * c + 8, :, :], part2[i][:, 0, :]).then_inc(s_stack[i], 16)
                if s.on(DIV):
                    sp.wait_ge(s_rec, s.n(DIV, 1, 1))
                    if s.b(DIV) >= 1:
                        settle(sp)
                        sp.wait_ge(s_yn, s.n(DIV, 1))
                    sp.dma_start(rec_dram.rearrange("k (c n) -> (k c) n", c=16), rec[:]).then_inc(s_recd, 16)
                if s.on(TURN):
                    sp.wait_ge(s_mt, s.n(TURN, 1, 1))
                    sp.dma_start(QS[s.b(TURN) % RING][MAXROW:MAXROW + 2, :, :], MpT[:]).then_inc(s_mrow, 16)
                if s.on(DIV):
                    sp.wait_ge(s_recd, s.n(DIV, 16, 16))
                    sp.dma_start(rden[:].rearrange("r a s -> r (a s)"),
                                 rec_dram.unsqueeze(1).broadcast_to([8, 16, NLO * S])).then_inc(s_shift, 16)
                if s.on(SPLIT):
                    sp.wait_ge(s_p3, s.n(SPLIT, 1, 1))
                    sp.dma_start(q[40:48, :, :], part3[i][:, 0, :]).then_inc(s_stack[i], 16)
                    sp.wait_ge(s_kp, s.n(SPLIT, 1, 1))
                    for r, n in ((0, 3), (24, 2), (40, 1)):
                        sp.dma_start(k[r:r + 8 * n].rearrange("r h v s -> r (h v s)"),
                                     kparts[i][0:32 * n].unsqueeze(1).broadcast_to([32 * n, 2, S]))\
                          .then_inc(s_stack[i], 16)
                if s.on(FFN) and s.b(FFN) % GRP == GRP - 1:
                    g = s.group(FFN + GRP - 1)
                    sp.wait_ge(s_fin, s.n(FFN, 1, 1))
                    settle(sp)
                    sp.dma_start(ov[bass.ds(g, 1)].rearrange("n p r d -> (n p) r d"), rows(g)).then_inc(s_store, 16)

            run_steps(sp, step)
            sp.wait_ge(s_store, 16 * (B // GRP))

        @block.gpsimd
        def _(gp):
            gp.memset(mhalf[:], -0.5)
            gp.memset(minus[:], -1.0)
            gp.memset(eps[:], EPS)
            gp.memset(zrow[:], 0.0).then_inc(s_setg, 1)
            gp.wait_ge(s_setg, 1)

            def inverse(s, lag, k):
                if not s.on(lag):
                    return
                gp.wait_ge(s_ln[k], s.n(lag, 2, 2))
                if s.b(lag) >= 1:
                    gp.wait_ge((s_xn1, s_a2, s_xn3, s_f2)[k], s.n(lag, 1))
                per = 3 if k in ON_ACT else 2
                if k in ON_ACT:
                    gp.tensor_tensor(nmean[k][:], mv[k][:, :, 0], minus[:], ALU.mult)
                gp.tensor_tensor(vareps[k][:], mv[k][:, :, 1], eps[:], ALU.add).then_inc(s_rstd[k], 1)
                gp.wait_ge(s_rstd[k], s.n(lag, per, 1))
                gp.tensor_tensor(rstd[k][:], vareps[k][:], mhalf[:], ALU.pow).then_inc(s_rstd[k], 1)
                if k in ON_ACT:
                    gp.wait_ge(s_rstd[k], s.n(lag, per, 2))
                    gp.tensor_tensor(shift[k][:], nmean[k][:], rstd[k][:], ALU.mult).then_inc(s_rstd[k], 1)

            def add_normed(s, lag, normed, done, added):
                if not s.on(lag):
                    return
                xs = X[:, bass.ds(s.n(lag, TT), TT), :]
                gp.wait_ge(done, s.n(lag, 1, 1))
                settle(gp)
                gp.tensor_tensor(xs, xs, normed[:], ALU.add).then_inc(added, 1)

            def step(s):
                inverse(s, MID, 2)
                if s.on(SPLIT):
                    gp.wait_ge(s_p2, s.n(SPLIT, 1, 1))
                    gp.tensor_tensor(part3[s.b(SPLIT) % 2][:], rest[:], part2[s.b(SPLIT) % 2][:],
                                     ALU.subtract).then_inc(s_p3, 1)
                inverse(s, OUT, 1)
                inverse(s, NORM, 0)
                add_normed(s, OUT, A2, s_a2, s_x1)
                inverse(s, FFN, 3)
                if s.on(DIV):
                    gp.wait_ge(s_shift, s.n(DIV, 16, 16))
                    if s.b(DIV) >= 1:
                        gp.wait_ge(s_op_ps, s.n(DIV, 1))
                    gp.tensor_tensor(yn[:], Y[:], rden[:], ALU.mult).then_inc(s_yn, 1)
                if s.on(PROJ):
                    gp.wait_ge(s_p1, s.n(PROJ, 1, 1))
                    if s.b(PROJ) >= 1:
                        gp.wait_ge(s_p3, s.n(PROJ, 1))
                    gp.tensor_tensor(rest[:], QK[:], part1[s.b(PROJ) % 2][:], ALU.subtract).then_inc(s_r1, 1)
                add_normed(s, FFN, F2, s_f2, s_fin)

            run_steps(gp, step)

        @block.scalar
        def _(act):
            def exp(s, n):
                if not s.on(ATT):
                    return
                banks = ST_CHUNKS[n][2]
                act.wait_ge(s_st_ps, s.n(ATT, CHUNKS, n + 1))
                if s.b(ATT) * CHUNKS + n >= 2:
                    act.wait_ge(s_pv, s.n(ATT, CHUNKS, n - 1))
                nc.scalar.activation(PT[n % 2][:, 0:512 * banks],
                                     ps_st[n % 2][:, 0:banks, :].rearrange("p a c -> p (a c)"),
                                     ACT.Exp, scale=SCALE).then_inc(s_exp, 1)

            def norm(s, lag, k, src, dst, done, added):
                if not s.on(lag):
                    return
                act.wait_ge(s_rstd[k], s.n(lag, 3, 3))
                if s.b(lag) >= 1:
                    act.wait_ge(added, s.n(lag, 1))
                for j in range(TT):
                    last = nc.scalar.activation(dst[:, j, :], src[:, j, :], ACT.Identity, bias=shift[k][:, j:j + 1],
                                                scale=rstd[k][:, j:j + 1])
                last.then_inc(done, 1)

            def step(s):
                if s.on(DIV):
                    act.wait_ge(s_pv, s.n(DIV, CHUNKS, CHUNKS))
                    if s.b(DIV) >= 1:
                        act.wait_ge(s_yn, s.n(DIV, 1))
                    nc.scalar.copy(Y[:], ps_y[:]).then_inc(s_y, 1)
                exp(s, 0)
                if s.on(SPLIT):
                    act.wait_ge(s_r1, s.n(SPLIT, 1, 1))
                    stacks_filled(act, s, SPLIT)
                    nc.scalar.copy(part2[s.b(SPLIT) % 2][:], rest[:]).then_inc(s_p2, 1)
                exp(s, 1)
                if s.on(TURN):
                    act.wait_ge(s_mt_ps, s.n(TURN, 1, 1))
                    if s.b(TURN) >= 1:
                        act.wait_ge(s_mrow, s.n(TURN, 16))
                    nc.scalar.copy(MpT[:].rearrange("r (n i) -> r i n", i=NB),
                                   ps_w[0:16, :].rearrange("r (i n) -> r i n", i=NB)).then_inc(s_mt, 1)
                exp(s, 2)
                if s.on(PROJ):
                    act.wait_ge(s_xt_ps, s.n(PROJ, 1, 1))
                    if s.b(PROJ) >= 1:
                        act.wait_ge(s_v_ps, s.n(PROJ, 1))
                    nc.scalar.copy(xn1T[:].rearrange("p (n i) -> p i n", i=NB),
                                   ps_w[:, 0:S].rearrange("p (i n) -> p i n", i=NB)).then_inc(s_xt, 1)
                if s.on(SPLIT):
                    i = s.b(SPLIT) % 2
                    act.wait_ge(s_p2, s.n(SPLIT, 1, 1))
                    act.wait_ge(s_p3, s.n(SPLIT, 1, 1))
                    for p, part in enumerate((part1[i], part2[i], part3[i])):
                        last = nc.scalar.copy(kparts[i][32 * p:32 * p + 32, :], part[32 * p:32 * p + 32, 1, :])
                    last.then_inc(s_kp, 1)
                exp(s, 3)
                norm(s, OUT, 1, A1, A2, s_a2, s_x1)
                if s.on(PROJ):
                    act.wait_ge(s_qk_ps, s.n(PROJ, 1, 1))
                    if s.b(PROJ) >= 1:
                        act.wait_ge(s_r1, s.n(PROJ, 1))
                    nc.scalar.activation(QK[:, 0, :], ps_w[:, 0:S], ACT.Identity, bias=bq_sb[:, 0:1]).then_inc(s_qk, 1)
                    nc.scalar.activation(QK[:, 1, :], ps_w[:, S:2 * S], ACT.Identity,
                                         bias=bk_sb[:, 0:1]).then_inc(s_qk, 1)
                exp(s, 4)
                if s.on(PROJ):
                    act.wait_ge(s_qk, s.n(PROJ, 2, 2))
                    stacks_filled(act, s, PROJ)
                    nc.scalar.copy(part1[s.b(PROJ) % 2][:], QK[:]).then_inc(s_p1, 1)
                if s.on(MID):
                    act.wait_ge(s_x3_ps, s.n(MID, 1, 1))
                    if s.b(MID) >= 1:
                        act.wait_ge(s_ff_ps, s.n(MID, 1))
                    nc.scalar.copy(xn3T[:], ps_w[:, 0:S]).then_inc(s_x3, 1)
                exp(s, 5)
                norm(s, FFN, 3, F1, F2, s_f2, s_fin)

            act.wait_ge(s_const, CONST)
            run_steps(act, step)

        @block.vector
        def _(dve):
            dve.memset(ones[:], 1.0).then_inc(s_wchain, 1)
            dve.wait_ge(s_const, CONST)
            nc.vector.tensor_copy(qfb[:], qf_sb[:]).then_inc(s_fix, 1)
            nc.vector.tensor_copy(kfb[:], kf_sb[:].rearrange("p v s -> p (v s)")).then_inc(s_fix, 1)
            nc.vector.tensor_copy(idb[:], id_sb[:]).then_inc(s_setup, 1)
            for i in range(RING):
                last = nc.vector.tensor_copy(VB[i][:, :, HD:2 * HD], vm_sb[:])
            last.then_inc(s_setup, 1)
            nc.vector.tensor_scalar(wneg[:], wf_sb[:], -1.0, None, ALU.mult).then_inc(s_wchain, 1)
            dve.wait_ge(s_wchain, 2)
            nc.vector.tensor_tensor(wabs[:], wf_sb[:], wneg[:], ALU.max).then_inc(s_wchain, 1)
            dve.wait_ge(s_wchain, 3)
            nc.vector.reduce_sum(wsum[:], wabs[:], AX_X).then_inc(s_setup, 1)
            dve.wait_ge(s_wps, 1)
            for j in range(TT):
                last = nc.vector.tensor_tensor(bo_sb[:, j, :], ps_w[:, 128:256], bo_sb[:, j, :], ALU.add)
            last.then_inc(s_bo, 1)
            dve.wait_ge(s_wps, 1)
            nc.vector.tensor_scalar(delta[:, 0:1], ps_w[:, 0:1], 1.0 / (D * D), 0.7, ALU.mult,
                                    ALU.mult).then_inc(s_wchain, 1)
            dve.wait_ge(s_wchain, 4)
            nc.vector.tensor_scalar(delta[:, 1:2], delta[:, 0:1], -1.0, None, ALU.mult).then_inc(s_wchain, 1)
            dve.wait_ge(s_wchain, 5)
            nc.vector.tensor_scalar(wabs[:], wf_sb[:], delta[:, 0:1], None, ALU.is_gt).then_inc(s_wchain, 1)
            nc.vector.tensor_scalar(wneg[:], wf_sb[:], delta[:, 1:2], None, ALU.is_lt).then_inc(s_wchain, 1)
            dve.wait_ge(s_wchain, 7)
            nc.vector.tensor_tensor(wneg[:], wabs[:], wneg[:], ALU.subtract).then_inc(s_wchain, 1)
            dve.wait_ge(s_wchain, 8)
            nc.vector.tensor_scalar(weff[:], wneg[:], al_sb[:, 0:1], None, ALU.mult).then_inc(s_weff, 1)

            dve.wait_ge(s_bo, 1)

            def spread(s, lag, k, src):
                if s.b(lag) >= 1:
                    dve.wait_ge(s_ln[k], s.n(lag, 2))
                for j in range(TT):
                    last = nc.vector.bn_stats(stats[k][:, j, :], src(j))
                last.then_inc(s_ln[k], 1)

            def moments(s, lag, k):
                if not s.on(lag):
                    return
                dve.wait_ge(s_ln[k], s.n(lag, 2, 1))
                if s.b(lag) >= 1:
                    dve.wait_ge((s_xn1, s_a2, s_xn3, s_f2)[k], s.n(lag, 1))
                settle(dve)
                for j in range(TT):
                    last = nc.vector.bn_aggr(mv[k][:, j, :], stats[k][:, j, :])
                last.then_inc(s_ln[k], 1)

            def norm(s, lag, k, src, dst, done):
                dve.wait_ge(s_rstd[k], s.n(lag, 2, 2))
                for j in range(TT):
                    last = nc.vector.tensor_scalar(dst[:, j, :], src(j), mv[k][:, j, 0:1], rstd[k][:, j:j + 1],
                                                   ALU.subtract, ALU.mult)
                last.then_inc(done, 1)

            def x_tile(s, lag):
                return lambda j: X[:, bass.ds(s.n(lag, TT, j), 1), :].rearrange("p a d -> p (a d)")

            def maxima(s, n):
                if not s.on(MAX):
                    return
                if n == 0 and s.b(MAX) >= 2:
                    dve.wait_ge(s_mp, s.n(MAX, 2, -2))
                dve.wait_ge(s_mx_ps, s.n(MAX, BANKS, n + 1))
                m = M[s.b(MAX) % 2][:].rearrange("p k g i -> p (k g) i")
                if MX_BANKS[n][0][1] == 1:
                    parts = [(2 * MX_BANKS[n][0][0], 4, 1)]
                else:
                    parts = [(2 * kv, 2, i) for kv, i in MX_BANKS[n]]
                at = 0
                for pair, pairs, i in parts:
                    w = pairs * BL * (i + 1)
                    last = nc.vector.tensor_reduce(
                        m[:, pair:pair + pairs, i],
                        ps_mx[n % 2][:, at:at + w].rearrange("p (h t) -> p h t", h=pairs), AX_X, ALU.max)
                    at += w
                last.then_inc(s_mx, 1)

            def step(s):
                if s.on(MID):
                    dve.wait_ge(s_x1, s.n(MID, 1, 1))
                    spread(s, MID, 2, x_tile(s, MID))
                if s.on(SPLIT):
                    dve.wait_ge(s_v_ps, s.n(SPLIT, 1, 1))
                    if s.b(SPLIT) >= RING:
                        dve.wait_ge(s_pv, s.n(SPLIT, CHUNKS, CHUNKS * (1 - RING)))
                    nc.vector.tensor_tensor(VB[s.b(SPLIT) % RING][:, :, 0:HD],
                                            ps_w[:, 0:128].rearrange("p (n c) -> p n c", c=HD), vm_sb[:],
                                            ALU.mult).then_inc(s_vb, 1)
                maxima(s, 0)
                if s.on(OUT):
                    dve.wait_ge(s_op_ps, s.n(OUT, 1, 1))
                    if s.b(OUT) >= 1:
                        dve.wait_ge(s_a2, s.n(OUT, 1))
                    nc.vector.tensor_tensor(A1[:], ps_w[:, 0:S].rearrange("p (j d) -> p j d", j=TT), bo_sb[:],
                                            ALU.add).then_inc(s_a1, 1)
                if s.on(TURN):
                    dve.wait_ge(s_mx, s.n(TURN, BANKS, BANKS))
                    if s.b(TURN) >= 1:
                        dve.wait_ge(s_mt_ps, s.n(TURN, 1))
                    m = M[s.b(TURN) % 2][:].rearrange("p k g i -> p (k g i)")
                    nc.vector.tensor_copy(Mp[:, 0, :], m).then_inc(s_mp, 1)
                moments(s, MID, 2)
                if s.on(TURN):
                    m = M[s.b(TURN) % 2][:].rearrange("p k g i -> p (k g i)")
                    dve.wait_ge(s_mp, s.n(TURN, 2, 1))
                    nc.vector.tensor_tensor(Mp[:, 1, :], m, Mp[:, 0, :], ALU.subtract).then_inc(s_mp, 1)
                maxima(s, 1)
                if s.on(OUT):
                    dve.wait_ge(s_a1, s.n(OUT, 1, 1))
                    spread(s, OUT, 1, lambda j: A1[:, j, :])
                maxima(s, 2)
                moments(s, OUT, 1)
                if s.on(DIV):
                    dve.wait_ge(s_den, s.n(DIV, 16, 16))
                    if s.b(DIV) >= 1:
                        dve.wait_ge(s_recd, s.n(DIV, 16))
                    nc.vector.reciprocal(rec[:], den[:]).then_inc(s_rec, 1)
                maxima(s, 3)
                if s.on(NORM):
                    if s.t0 % GRP == 0:
                        dve.wait_ge(s_x, (s.group(0) + 1) * 16)
                    spread(s, NORM, 0, x_tile(s, NORM))
                maxima(s, 4)
                if s.on(FFN):
                    dve.wait_ge(s_ff_ps, s.n(FFN, 1, 1))
                    if s.b(FFN) >= 1:
                        dve.wait_ge(s_f2, s.n(FFN, 1))
                    nc.vector.tensor_tensor(F1[:], ps_w[:, 0:S].rearrange("p (j d) -> p j d", j=TT), bf_sb[:],
                                            ALU.add).then_inc(s_f1, 1)
                moments(s, NORM, 0)
                if s.on(FFN):
                    dve.wait_ge(s_f1, s.n(FFN, 1, 1))
                    spread(s, FFN, 3, lambda j: F1[:, j, :])
                maxima(s, 5)
                moments(s, FFN, 3)
                if s.on(MID):
                    if s.b(MID) >= 1:
                        dve.wait_ge(s_x3_ps, s.n(MID, 1))
                    norm(s, MID, 2, x_tile(s, MID), xn3, s_xn3)
                maxima(s, 6)
                maxima(s, 7)
                if s.on(NORM):
                    if s.b(NORM) >= 1:
                        dve.wait_ge(s_xt_ps, s.n(NORM, 1))
                    norm(s, NORM, 0, x_tile(s, NORM), xn1, s_xn1)
                maxima(s, 8)
                maxima(s, 9)

            run_steps(dve, step)

        @block.tensor
        def _(pe):
            pe.wait_ge(s_const, CONST)
            for lo in range(NLO):
                pe.matmul(ps_w[:, 128:256], bv_sb[:, lo, :], wo_sb[:, lo, :], start=(lo == 0), stop=(lo == NLO - 1))
            pe.wait_ge(s_setup, 3)
            pe.wait_ge(s_wchain, 1)
            pe.matmul(ps_w[:, 0:1], ones[:], wsum[:], start=True, stop=True).then_inc(s_wps, 1)
            pe.wait_ge(s_weff, 1)
            pe.wait_ge(s_bo, 1)

            def take(s, user):
                sm, v = last_work(s, user)
                if sm is not None:
                    pe.wait_ge(sm, v)

            def st(s, n):
                if not s.on(ATT):
                    return
                if n == 0:
                    pe.wait_ge(s_mrow, s.n(ATT, 16, 16))
                if s.b(ATT) * CHUNKS + n >= 2:
                    pe.wait_ge(s_exp, s.n(ATT, CHUNKS, n - 1))
                lo, mats, _ = ST_CHUNKS[n]
                q = QS[s.b(ATT) % RING][:].rearrange("p h (s j) -> p j h s", j=NB)
                k = KS[s.b(ATT) % RING][:].rearrange("p k v (s i) -> p k v i s", i=NB)
                dst = ps_st[n % 2][:].rearrange("p a c -> p (a c)")
                for i, diag, j, nj, slot in mats:
                    for hi in range(2):
                        h = hi * 8 + lo * G
                        last = pe.matmul(dst[64 * hi:64 * hi + 64, SLOT * slot:SLOT * (slot + nj)],
                                         k[:, 2 * hi + lo, 0 if diag else 1, i, :], q[:, j:j + nj, h:h + G, :],
                                         start=True, stop=True, skip_group_check=True)
                last.then_inc(s_st_ps, 1)

            def pv(s, n):
                if not s.on(ATT):
                    return
                lo = ST_CHUNKS[n][0]
                pe.wait_ge(s_exp, s.n(ATT, CHUNKS, n + 1))
                if n == 0:
                    pe.wait_ge(s_vb, s.n(ATT, 1, 1))
                    if s.b(ATT) >= 1:
                        pe.wait_ge(s_y, s.n(ATT, 1))
                v = VB[s.b(ATT) % RING]
                p = PT[n % 2][:].rearrange("p (j g s) -> p g j s", g=G, s=BL)
                for i, slot in PV_CHUNKS[n]:
                    at = 2 * (NLO * i + lo)
                    for g in range(G):
                        last = pe.matmul(ps_y[32 * g:32 * g + 32, lo, BL * i:S],
                                         v[:, at:at + 2, :].rearrange("p a c -> p (a c)"),
                                         p[:, g, slot:slot + NB - i, :], start=(i == 0), stop=(i == 2))
                last.then_inc(s_pv, 1)

            def mx(s, n):
                if not s.on(MAX):
                    return
                b = s.b(MAX)
                if n == 0:
                    v = (b // 2 + 1) * STACK
                    pe.wait_ge(s_stack[b % 2], v if s.it is None else s.it * (2 * STACK) + v)
                if b * BANKS + n >= 2:
                    pe.wait_ge(s_mx, s.n(MAX, BANKS, n - 1))
                q = QS[b % RING][:].rearrange("p h s -> p (h s)")
                k = KS[b % RING][:].rearrange("p k v (s i) -> p k v s i", i=NB)
                at = 0
                for kv, i in MX_BANKS[n]:
                    for pair in range(2):
                        h = kv * G + 2 * pair
                        queries = q[:, h * S + i:(h + 2) * S:NB]
                        last = pe.matmul(ps_mx[n % 2][:, at:at + BL], queries, k[:, kv, 0, :, i],
                                         start=True, stop=True, skip_group_check=True)
                        at += BL
                        if i:
                            last = pe.matmul(ps_mx[n % 2][:, at:at + BL * i], queries, k[:, kv, 1, :, 0:i],
                                             start=True, stop=True, skip_group_check=True)
                            at += BL * i
                last.then_inc(s_mx_ps, 1)

            def step(s):
                if s.on(SPLIT):
                    pe.wait_ge(s_xt, s.n(SPLIT, 1, 1))
                    take(s, "v")
                    for i in range(NB):
                        for hi in range(2):
                            last = pe.matmul(ps_w[64 * hi:64 * hi + 64, 32 * i:32 * i + 32],
                                             xn1T[:, i:S:NB], wv_sb[:], start=True,
                                             stop=True, skip_group_check=True)
                    last.then_inc(s_v_ps, 1)
                st(s, 0)
                mx(s, 0)
                if s.on(OUT):
                    pe.wait_ge(s_yn, s.n(OUT, 1, 1))
                    take(s, "op")
                    for j in range(TT):
                        for lo in range(NLO):
                            last = pe.matmul(ps_w[:, D * j:D * j + D], yn[:, lo, 128 * j:128 * j + 128],
                                             wo_sb[:, lo, :], start=(lo == 0), stop=(lo == NLO - 1))
                    last.then_inc(s_op_ps, 1)
                mx(s, 1)
                st(s, 1)
                pv(s, 0)
                mx(s, 2)
                if s.on(TURN):
                    pe.wait_ge(s_mp, s.n(TURN, 2, 2))
                    take(s, "turn")
                    parts = Mp[:].rearrange("p a (c i) -> p i (a c)", i=NB)
                    for i in range(NB):
                        last = pe.matmul(ps_w[0:16, 128 * i:128 * i + 128], parts[:, i, :], idb[:], start=True,
                                         stop=True, skip_group_check=True)
                    last.then_inc(s_mt_ps, 1)
                mx(s, 3)
                st(s, 2)
                pv(s, 1)
                if s.on(PROJ):
                    pe.wait_ge(s_xn1, s.n(PROJ, 1, 1))
                    take(s, "x1")
                    for j in range(TT):
                        last = pe.transpose(ps_w[:, 128 * j:128 * j + 128], xn1[:, j, :], id_sb[:])
                    last.then_inc(s_xt_ps, 1)
                mx(s, 4)
                st(s, 3)
                pv(s, 2)
                if s.on(FFN):
                    pe.wait_ge(s_x3, s.n(FFN, 1, 1))
                    take(s, "ff")
                    for j in range(TT):
                        last = pe.matmul(ps_w[:, D * j:D * j + D], xn3T[:, 128 * j:128 * j + 128], weff[:],
                                         start=True, stop=True)
                    last.then_inc(s_ff_ps, 1)
                mx(s, 5)
                if s.on(PROJ):
                    pe.wait_ge(s_xt, s.n(PROJ, 1, 1))
                    take(s, "qk")
                    pe.matmul(ps_w[:, 0:S], wq_sb[:], xn1T[:], start=True, stop=True)
                    pe.matmul(ps_w[:, S:2 * S], wk_sb[:], xn1T[:], start=True, stop=True).then_inc(s_qk_ps, 1)
                mx(s, 6)
                st(s, 4)
                pv(s, 3)
                mx(s, 7)
                if s.on(MID):
                    pe.wait_ge(s_xn3, s.n(MID, 1, 1))
                    take(s, "x3")
                    for j in range(TT):
                        last = pe.transpose(ps_w[:, 128 * j:128 * j + 128], xn3[:, j, :], id_sb[:])
                    last.then_inc(s_x3_ps, 1)
                mx(s, 8)
                st(s, 5)
                pv(s, 4)
                mx(s, 9)
                pv(s, 5)

            run_steps(pe, step)


def kernel(**inputs):
    import numpy as np
    import concourse.bacc as bacc
    from concourse.bass_utils import run_bass_kernel_spmd

    f = np.float32
    w_qkv = np.ascontiguousarray(inputs["L0_attn_W_qkv"])
    b_qkv = np.ascontiguousarray(inputs["L0_attn_b_qkv"])
    wq = w_qkv[:, :128].reshape(D, NH, HD).transpose(0, 2, 1).reshape(D, 128)
    bq = b_qkv[:128].reshape(NH, HD).T.reshape(128, 1)
    wk = w_qkv[:, 128:160].reshape(D, NKV, HD).transpose(0, 2, 1).reshape(D, 32)
    bk = b_qkv[128:160].reshape(NKV, HD).T.reshape(32, 1)
    wv = w_qkv[:, 160:].reshape(D, 2, NLO, HD).transpose(0, 2, 1, 3).reshape(D, 32)
    wo = np.zeros((G, 2, 2, HD, NLO, D), f)
    wo[:, :, 0] = np.asarray(inputs["L0_attn_W_out"]).reshape(2, NLO, G, HD, D).transpose(2, 0, 3, 1, 4)
    bvw = np.zeros((G, 2, 2, HD, NLO, 128), f)
    bvw[:, :, 0] = b_qkv[160:].reshape(2, NLO, HD).transpose(0, 2, 1)[None, :, :, :, None]
    qfix = np.zeros((128, BL), f)
    qfix[64:] = np.arange(BL)[None, :] < np.arange(BL)[:, None]
    kfix = np.zeros((128, 2, BL), f)
    kfix[64:, 0] = -BIG * np.eye(BL, dtype=f)
    kfix[MAXROW:MAXROW + 2] = -1.0
    half = (np.arange(128)[:, None] // 64 == np.arange(2)[None, :]).astype(f)
    arrays = {
        "x": inputs["L0_attn_x"],
        "wq": wq, "wk": np.tile(wk, (1, 4)), "wv": wv, "wo": wo.reshape(128, NLO, D),
        "bq": bq, "bk": np.tile(bk, (4, 1)),
        "bo": np.broadcast_to(np.asarray(inputs["L0_attn_b_out"]), (128, TT, D)),
        "wf": np.asarray(inputs["L0_ffn_weight"]).T,
        "alpha": np.broadcast_to(np.asarray(inputs["L0_ffn_alpha"]), (128, 1)),
        "bf": np.broadcast_to(np.asarray(inputs["L0_ffn_bias"]), (128, TT, D)),
        "ident": np.eye(128, dtype=f), "qfix": np.repeat(qfix, NB, 1), "kfix": np.repeat(kfix, NB, 2),
        "vmask": np.broadcast_to(half[:, None, :, None], (128, NB * NLO, 2, HD)).reshape(128, -1, HD),
        "bvw": bvw.reshape(128, NLO, 128),
    }
    arrays = {f"in_{k}": np.ascontiguousarray(v) for k, v in arrays.items()}
    nc = bacc.Bacc("TRN2", target_bir_lowering=False, num_devices=1)
    args = [nc.dram_tensor(k, v.shape, mybir.dt.from_np(v.dtype), kind="ExternalInput").ap()
            for k, v in arrays.items()]
    names = ["x", "wq", "wk", "wv", "wo", "bq", "bk", "bo", "wf", "alpha", "bf", "ident", "qfix", "kfix", "vmask",
             "bvw"]
    args = dict(zip(arrays, args))
    o = nc.dram_tensor("out", (B, S, D), F32, kind="ExternalOutput").ap()
    build(nc, *[args[f"in_{k}"] for k in names], o)
    got = run_bass_kernel_spmd(nc, [arrays], core_ids=[0])
    return got.results[0]["out"]
```
